# Optimizing a Trainium2 kernel written in Bass

```python
import numpy as np
import jax
import jax.numpy as jnp

def _softmax(x, axis=-1):
    return jax.nn.softmax(x, axis=axis)

def _gelu(x):
    return jax.nn.gelu(x, approximate=True)

def _silu(x):
    return jax.nn.silu(x)

def _sigmoid(x):
    return jax.nn.sigmoid(x)

def _layernorm(x, axis=-1, eps=1e-05):
    m = jnp.mean(x, axis=axis, keepdims=True)
    v = jnp.var(x, axis=axis, keepdims=True)
    return (x - m) / jnp.sqrt(v + eps)

def _scatter_add(tgt, idx, src, axis=0):
    return tgt.at[idx].add(src)

def _segment_sum(src, seg, n):
    return jax.ops.segment_sum(src, seg, n)
kernel_name = 'mk_adaln_ffn_d1_seqx_r4_e3015e'

def setup_inputs(seed: int=0):
    np.random.seed(seed)
    _w = jnp.asarray

    def _rec_inputs():
        import jax
        import jax.numpy as jnp
        _rk = jax.random.key(seed)
        x = -7.109e-05 + 0.9999 * jax.random.normal(jax.random.fold_in(_rk, 1), (64, 64, 1024), jnp.float32)
        _lenS = 64 - jax.random.randint(jax.random.fold_in(_rk, 7), (64,), 0, max(1, 64 // 4) + 1, jnp.int32)
        _lenS2 = 64 - jax.random.randint(jax.random.fold_in(_rk, 8), (64,), 0, max(1, 64 // 4) + 1, jnp.int32)
        itok_B_0_15 = jax.random.randint(jax.random.fold_in(_rk, 11), (64,), 0, 16, jnp.int32)
        return (x, itok_B_0_15)
    x, itok_B_0_15 = _rec_inputs()

    def _L0_cond_setup():
        import jax, jax.numpy as jnp
        import numpy as np
        NUM_CONDITIONS = 16
        IN_CH = 64
        OUT_CH = 64
        B = 64
        T = 1024
        key = jax.random.key(seed)
        k_x, k_w, k_c = jax.random.split(key, 3)
        x = jax.random.normal(k_x, (B, IN_CH, T), dtype=jnp.float32)
        bound = float(np.sqrt(6.0 / IN_CH))
        weights = jax.random.uniform(k_w, (NUM_CONDITIONS, IN_CH, OUT_CH), dtype=jnp.float32, minval=-bound, maxval=bound)
        condition = jax.random.randint(k_c, (B,), 0, NUM_CONDITIONS, dtype=jnp.int64)
        return {'x': x, 'weights': weights, 'condition': condition}
    _L0_cond_all = _L0_cond_setup()
    _L0_cond_in = {k: v for k, v in _L0_cond_all.items() if k in ('weights',)}
    del _L0_cond_all

    def _L0_ffn_setup():
        import jax, jax.numpy as jnp
        import numpy as np
        B, S, D_IN, D_OUT = (2, 512, 1024, 1024)
        E, K, R = (8, 2, 16)
        SCALING = 32.0 / 16.0
        key = jax.random.key(seed)
        ks = jax.random.split(key, 6)
        x = jax.random.normal(ks[0], (B, S, D_IN), dtype=jnp.float32)
        gate_w = jax.random.normal(ks[1], (E, D_IN), dtype=jnp.float32) * 0.02
        base_w = jax.random.normal(ks[2], (D_OUT, D_IN), dtype=jnp.float32) * 0.02
        base_b = jax.random.normal(ks[3], (D_OUT,), dtype=jnp.float32) * 0.02
        lora_A = jax.random.normal(ks[4], (E, R, D_IN), dtype=jnp.float32) * 0.02
        lora_B = jax.random.normal(ks[5], (E, D_OUT, R), dtype=jnp.float32) * 0.02
        return {'x': x, 'gate_w': gate_w, 'base_w': base_w, 'base_b': base_b, 'lora_A': lora_A, 'lora_B': lora_B}
    _L0_ffn_all = _L0_ffn_setup()
    _L0_ffn_in = {k: v for k, v in _L0_ffn_all.items() if k in ('gate_w', 'base_w', 'base_b', 'lora_A', 'lora_B')}
    del _L0_ffn_all
    return {'x': x, 'itok_B_0_15': itok_B_0_15, 'L0_cond_weights': _L0_cond_in['weights'], 'L0_ffn_gate_w': _L0_ffn_in['gate_w'], 'L0_ffn_base_w': _L0_ffn_in['base_w'], 'L0_ffn_base_b': _L0_ffn_in['base_b'], 'L0_ffn_lora_A': _L0_ffn_in['lora_A'], 'L0_ffn_lora_B': _L0_ffn_in['lora_B']}

def reference(x, itok_B_0_15, L0_cond_weights, L0_ffn_gate_w, L0_ffn_base_w, L0_ffn_base_b, L0_ffn_lora_A, L0_ffn_lora_B):
    import jax
    import jax.numpy as jnp

    def _L0_cond_ref(x, weights, condition):
        import jax, jax.numpy as jnp
        import numpy as np
        NUM_CONDITIONS = 16
        IN_CH = 64
        OUT_CH = 64
        B = 64
        T = 1024
        W = weights[condition]
        return jnp.einsum('bct,bcd->bdt', x, W)

    def _L0_ffn_ref(x, gate_w, base_w, base_b, lora_A, lora_B):
        import jax, jax.numpy as jnp
        import numpy as np
        B, S, D_IN, D_OUT = (2, 512, 1024, 1024)
        E, K, R = (8, 2, 16)
        SCALING = 32.0 / 16.0
        gate_logits = jnp.einsum('bsd,ed->bse', x, gate_w)
        weights, selected = jax.lax.top_k(gate_logits, K)
        weights = jax.nn.softmax(weights.astype(jnp.float32), axis=2).astype(x.dtype)
        result = jnp.einsum('bsd,od->bso', x, base_w) + base_b
        w_full = jnp.sum(jax.nn.one_hot(selected, E, dtype=x.dtype) * weights[..., None], axis=2)
        low = jnp.einsum('bsd,erd->ebsr', x, lora_A)
        lora_out = jnp.einsum('ebsr,eor,bse->bso', low, lora_B, w_full)
        result = result + SCALING * lora_out
        return result
    x = x + _L0_ffn_ref(_L0_cond_ref(x, L0_cond_weights, itok_B_0_15), L0_ffn_gate_w, L0_ffn_base_w, L0_ffn_base_b, L0_ffn_lora_A, L0_ffn_lora_B)
    return x

_drawn_inputs = setup_inputs


def setup_inputs(seed=0):
    import zlib

    import numpy as np

    out = dict(_drawn_inputs(seed))
    spreads = {}
    factors = {'L0_ffn_base_b': 4.057}
    for name, (base, spread) in spreads.items():
        noise = np.random.default_rng([zlib.crc32(name.encode()), seed]).standard_normal(out[name].shape)
        drawn = base * np.exp(spread * noise) if base else spread * noise
        out[name] = jnp.asarray(drawn.astype(out[name].dtype))
    for name, factor in factors.items():
        out[name] = (out[name] * factor).astype(out[name].dtype)
    return out
```

```python
from contextlib import ExitStack

import concourse.bass as bass
from concourse import mybir

ALU = mybir.AluOpType
ACT = mybir.ActivationFunctionType
F32 = mybir.dt.float32
F32R = mybir.dt.float32r
I32 = mybir.dt.int32
U32 = mybir.dt.uint32

AX_X = mybir.AxisListType.X

P = 128
TOP_K = 2
SCALING = 32.0 / 16.0


def adaln_ffn_kernel(
    nc: bass.Bass,
    x: bass.AP,
    condition: bass.AP,
    cond_w: bass.AP,
    proj_w: bass.AP,
    lora_b: bass.AP,
    base_b: bass.AP,
    out: bass.AP,
):
    B, CH, T = x.shape
    O = out.shape[2]
    ER = lora_b.shape[0]
    N = proj_w.shape[1]
    NE = N - O - ER
    RANK = ER // NE
    KT = T // P
    PAIRS = B * CH // P
    HALF_K = KT // 2
    assert 2 * CH == P and ER == P and KT % 2 == 0 and PAIRS % 2 == 0 and O % 8 == 0

    BW = (N + 2) // 3 + (N + 2) // 3 % 2
    BANKS = [(0, BW), (BW, 2 * BW), (2 * BW, N)]
    TAIL = O - 2 * BW
    RANKS = (TAIL, TAIL + ER)
    GATES = (TAIL + ER, TAIL + ER + NE)
    STAGES = 3

    x_pairs = x.rearrange("(n two) c t -> n (two c) t", two=2)
    out_pairs = out.rearrange("(n two) c o -> n (two c) o", two=2)

    with ExitStack() as ctx:
        def sb(name, shape, dt):
            return ctx.enter_context(nc.sbuf_tensor(name, shape, dt))

        def sem(name):
            return ctx.enter_context(nc.semaphore(name))

        w_raw = sb("w_raw", [P, STAGES, N], F32)
        w_hi = sb("w_hi", [P, KT, N], F32R)
        w_lo = sb("w_lo", [P, KT, N], F32R)
        lb_raw = sb("lb_raw", [P, O], F32)
        lb_hi = sb("lb_hi", [P, O], F32R)
        lb_lo = sb("lb_lo", [P, O], F32R)
        bias = sb("bias", [P, O], F32)
        cw_raw = sb("cw_raw", [P, cond_w.shape[1]], F32)
        cw_parts = sb("cw_parts", [P, 2, cond_w.shape[1]], F32R)
        cond_sb = sb("cond_sb", [1, B], I32)
        ident = sb("ident", [P, P], F32)
        earlier = sb("earlier", [P, NE, NE], F32)

        x_sb = sb("x_sb", [P, 2, T], F32)
        x_parts = sb("x_parts", [P, 2, 2, T], F32R)
        w_sel = sb("w_sel", [P, 2, 2, 2, CH], F32R)
        y_hi = sb("y_hi", [P, 2, KT, P], F32R)
        y_lo = sb("y_lo", [P, 2, KT, P], F32R)
        res = sb("res", [P, 2, O], F32)
        logits_sb = sb("logits_sb", [P, NE], F32)
        top = sb("top", [P, 1], F32)
        below = sb("below", [P, NE], F32)
        exps = sb("exps", [P, NE], F32)
        greater = sb("greater", [P, NE, NE], F32)
        ties = sb("ties", [P, NE, NE], F32)
        rank = sb("rank", [P, NE], F32)
        chosen = sb("chosen", [P, NE], F32)
        sum_exps = sb("sum_exps", [P, 1], F32)
        scale = sb("scale", [P, 1], F32)
        gate = sb("gate", [P, NE], F32)
        low = sb("low", [P, ER], F32)
        lowT_hi = sb("lowT_hi", [P, P], F32R)
        lowT_lo = sb("lowT_lo", [P, P], F32R)

        acc = ctx.enter_context(nc.psum_tensor("acc", [P, 2, 3, 512], F32))
        mixed = ctx.enter_context(nc.psum_tensor("mixed", [P, 2, 512], F32))

        cond_in = sem("cond_in")
        cw_in = sem("cw_in")
        w_in = [sem(f"w_in{i}") for i in range(STAGES)]
        lb_in = sem("lb_in")
        bias_in = sem("bias_in")
        cw_hi_ready = sem("cw_hi_ready")
        cw_ready = sem("cw_ready")
        w_hi_ready = sem("w_hi_ready")
        w_ready = sem("w_ready")
        lb_hi_ready = sem("lb_hi_ready")
        lb_ready = sem("lb_ready")
        ident_zero = sem("ident_zero")
        consts_ready = sem("consts_ready")
        x_in = [sem("x_in0"), sem("x_in1")]
        stored = [sem("stored0"), sem("stored1")]
        x_hi_ready = sem("x_hi_ready")
        x_split = sem("x_split")
        sel_ready = sem("sel_ready")
        mix_done = sem("mix_done")
        y_hi_ready = sem("y_hi_ready")
        y_ready = sem("y_ready")
        proj_done = sem("proj_done")
        logits_ready = sem("logits_ready")
        top_ready = sem("top_ready")
        below_ready = sem("below_ready")
        exp_ready = sem("exp_ready")
        compared = sem("compared")
        ties_ready = sem("ties_ready")
        ahead_ready = sem("ahead_ready")
        rank_ready = sem("rank_ready")
        chosen_ready = sem("chosen_ready")
        sum_exps_ready = sem("sum_exps_ready")
        scale_ready = sem("scale_ready")
        gate_ready = sem("gate_ready")
        low_ready = sem("low_ready")
        lowT_done = sem("lowT_done")
        lowT_hi_ready = sem("lowT_hi_ready")
        lowT_ready = sem("lowT_ready")
        lora_done = sem("lora_done")
        sum_ready = sem("sum_ready")
        res_ready = sem("res_ready")

        block = ctx.enter_context(nc.Block())

        LOOPS = (PAIRS - 4) // 2

        @block.sync
        def _(sp):
            sp.dma_start(cond_sb[:, :], condition).then_inc(cond_in, 16)
            for half in range(2):
                sp.dma_start(cw_raw[half * CH:(half + 1) * CH, :], cond_w).then_inc(cw_in, 16)

            def load_x(j, c):
                sp.dma_start(x_sb[:, c % 2, :], x_pairs[2 * j + c]).then_inc(x_in[c % 2], 16)

            load_x(0, 0)
            for k in range(KT):
                if k >= STAGES:
                    sp.wait_ge(w_hi_ready, k - STAGES + 1)
                    sp.wait_ge(w_ready, k - STAGES + 1)
                sp.dma_start(w_raw[:, k % STAGES, :], proj_w[k * P:(k + 1) * P, :]).then_inc(w_in[k % STAGES], 16)
                if k == 0:
                    load_x(0, 1)
            sp.dma_start(bias[:, :], base_b.partition_broadcast(P)).then_inc(bias_in, 16)
            sp.dma_start(lb_raw[:, :], lora_b).then_inc(lb_in, 16)

            def step(j, c, first=False, last=False):
                s = 2 * j + c
                if not last:
                    sp.wait_ge(x_split, s + 1)
                    sp.wait_ge(sum_ready, s + 1)
                    load_x(j, c + 2)
                if not first:
                    store(j, c - 1)

            def store(j, c):
                sp.wait_ge(res_ready, 2 * j + c + 1)
                sp.dma_start(out_pairs[2 * j + c], res[:, c % 2, :]).then_inc(stored[c % 2], 16)

            step(0, 0, first=True)
            step(0, 1)
            with sp.Fori(0, LOOPS) as j:
                for u in (2, 3):
                    step(j, u)
            for s in (PAIRS - 2, PAIRS - 1):
                step(0, s, last=True)
            store(0, PAIRS - 1)
            for i in range(2):
                sp.wait_ge(stored[i], 16 * (PAIRS // 2))

        @block.gpsimd
        def _(pool):
            nc.gpsimd.memset(ident[:, :], 0.0).then_inc(ident_zero, 1)
            nc.gpsimd.memset(earlier[:, :, :], 0.0).then_inc(ident_zero, 1)
            pool.wait_ge(ident_zero, 2)
            for e in range(1, NE):
                nc.gpsimd.memset(earlier[:, e, 0:e], 1.0)
            nc.gpsimd.affine_select(out=ident[:, :], in_=ident[:, :], compare_op=ALU.not_equal, fill=1.0, base=0,
                                    pattern=[[-1, P]], channel_multiplier=1).then_inc(consts_ready, 1)

            def select(j, c):
                if c >= 2:
                    pool.wait_ge(mix_done, 2 * (2 * j + c) - 2)
                for b in range(2):
                    cond = pool.value_load(cond_sb[0:1, bass.ds(4 * j + 2 * c + b, 1)], min_val=0, max_val=15)
                    last = nc.gpsimd.tensor_copy(w_sel[:, c % 2, b, :, :], cw_parts[:, :, bass.ds(cond * CH, CH)])
                last.then_inc(sel_ready, 1)

            def add_bias(j, c):
                if c >= 2:
                    pool.wait_ge(stored[c % 2], 16 * (j + c // 2))
                pool.wait_ge(x_in[c % 2], 16 * (j + c // 2 + 1))
                nc.gpsimd.tensor_tensor(res[:, c % 2, :], x_sb[:, c % 2, :], bias[:, :], ALU.add).then_inc(sum_ready, 1)

            pool.wait_ge(cond_in, 16)
            pool.wait_ge(cw_ready, 1)
            select(0, 0)
            select(0, 1)
            pool.wait_ge(bias_in, 16)
            add_bias(0, 0)
            select(0, 2)
            add_bias(0, 1)
            select(0, 3)
            with pool.Fori(0, LOOPS) as j:
                for u in (2, 3):
                    add_bias(j, u)
                    select(j, u + 2)
            add_bias(0, PAIRS - 2)
            add_bias(0, PAIRS - 1)

        @block.scalar
        def _(act):
            def x_high(j, c):
                if c >= 2:
                    act.wait_ge(mix_done, 2 * (2 * j + c) - 2)
                act.wait_ge(x_in[c % 2], 16 * (j + c // 2 + 1))
                nc.scalar.copy(x_parts[0:CH, c % 2, 0, :], x_sb[0:CH, c % 2, :])
                nc.scalar.copy(x_parts[CH:P, c % 2, 1, :], x_sb[CH:P, c % 2, :]).then_inc(x_hi_ready, 1)

            def y_high(j, c):
                if c >= 2:
                    act.wait_ge(proj_done, 2 * j + c - 1)
                for h in range(2):
                    act.wait_ge(mix_done, 2 * (2 * j + c) + h + 1)
                    nc.scalar.copy(y_hi[:, c % 2, h * HALF_K:(h + 1) * HALF_K, :],
                                   mixed[:, h, :].rearrange("p (k m) -> p k m", m=P)).then_inc(y_hi_ready, 1)

            def gate_exp(j, c):
                act.wait_ge(below_ready, 2 * j + c + 1)
                nc.scalar.activation(exps[:, :], below[:, :], ACT.Exp).then_inc(exp_ready, 1)

            def lowT_high(j, c):
                act.wait_ge(lowT_done, 2 * j + c + 1)
                if c >= 1:
                    act.wait_ge(lora_done, 2 * j + c)
                nc.scalar.copy(lowT_hi[:, :], mixed[:, 0, 0:P]).then_inc(lowT_hi_ready, 1)

            act.wait_ge(cw_in, 32)
            nc.scalar.copy(cw_parts[:, 0, :], cw_raw[:, :]).then_inc(cw_hi_ready, 1)
            x_high(0, 0)
            y_high(0, 0)
            for k in range(KT):
                act.wait_ge(w_in[k % STAGES], 16 * (k // STAGES + 1))
                nc.scalar.copy(w_hi[:, k, :], w_raw[:, k % STAGES, :]).then_inc(w_hi_ready, 1)
                if k == 0:
                    x_high(0, 1)
            act.wait_ge(lb_in, 16)
            nc.scalar.copy(lb_hi[:, :], lb_raw[:, :]).then_inc(lb_hi_ready, 1)

            def step(j, c, first=False, last=0):
                if not first:
                    gate_exp(j, c - 1)
                    lowT_high(j, c - 1)
                if last < 2:
                    y_high(j, c + 1)
                if last < 1:
                    x_high(j, c + 2)

            step(0, 0, first=True)
            step(0, 1)
            with act.Fori(0, LOOPS) as j:
                for u in (2, 3):
                    step(j, u)
            step(0, PAIRS - 2, last=1)
            step(0, PAIRS - 1, last=2)
            gate_exp(0, PAIRS - 1)
            lowT_high(0, PAIRS - 1)

        @block.vector
        def _(dve):
            def x_low(j, c):
                dve.wait_ge(x_hi_ready, 2 * j + c + 1)
                nc.vector.tensor_tensor(x_parts[CH:P, c % 2, 0, :], x_sb[0:CH, c % 2, :],
                                        x_parts[0:CH, c % 2, 0, :].bitcast(F32), ALU.subtract)
                nc.vector.tensor_tensor(x_parts[0:CH, c % 2, 1, :], x_sb[CH:P, c % 2, :],
                                        x_parts[CH:P, c % 2, 1, :].bitcast(F32), ALU.subtract).then_inc(x_split, 1)

            def y_low(j, c):
                for h in range(2):
                    dve.wait_ge(y_hi_ready, 2 * (2 * j + c) + h + 1)
                    ks = slice(h * HALF_K, (h + 1) * HALF_K)
                    nc.vector.tensor_tensor(y_lo[:, c % 2, ks, :], mixed[:, h, :].rearrange("p (k m) -> p k m", m=P),
                                            y_hi[:, c % 2, ks, :].bitcast(F32), ALU.subtract).then_inc(y_ready, 1)

            def gating(j, c):
                n = 2 * j + c + 1
                logits = logits_sb[:, :]
                here = logits.unsqueeze(2).broadcast_to([P, NE, NE])
                other = logits.unsqueeze(1).broadcast_to([P, NE, NE])
                dve.wait_ge(proj_done, n)
                nc.vector.tensor_copy(logits_sb[:, :], acc[:, c % 2, 2, GATES[0]:GATES[1]]).then_inc(logits_ready, 1)
                dve.wait_ge(logits_ready, n)
                nc.vector.reduce_max(top[:, :], logits, AX_X).then_inc(top_ready, 1)
                nc.vector.tensor_tensor(ties[:, :, :], other, here, ALU.is_equal).then_inc(compared, 1)
                dve.wait_ge(top_ready, n)
                nc.vector.tensor_scalar(below[:, :], logits, top[:, :], None, ALU.subtract).then_inc(below_ready, 1)
                nc.vector.tensor_tensor(greater[:, :, :], other, here, ALU.is_gt).then_inc(compared, 1)
                dve.wait_ge(compared, 2 * n)
                nc.vector.tensor_tensor(ties[:, :, :], ties[:, :, :], earlier[:, :, :], ALU.mult) \
                    .then_inc(ties_ready, 1)
                dve.wait_ge(ties_ready, n)
                nc.vector.tensor_tensor(greater[:, :, :], greater[:, :, :], ties[:, :, :], ALU.add) \
                    .then_inc(ahead_ready, 1)
                dve.wait_ge(ahead_ready, n)
                nc.vector.reduce_sum(rank[:, :], greater[:, :, :], AX_X).then_inc(rank_ready, 1)
                dve.wait_ge(rank_ready, n)
                dve.wait_ge(exp_ready, n)
                nc.vector.scalar_tensor_tensor(out=chosen[:, :], in0=rank[:, :], scalar=float(TOP_K), in1=exps[:, :],
                                               op0=ALU.is_lt, op1=ALU.mult).then_inc(chosen_ready, 1)
                dve.wait_ge(chosen_ready, n)
                nc.vector.reduce_sum(sum_exps[:, :], chosen[:, :], AX_X).then_inc(sum_exps_ready, 1)
                dve.wait_ge(sum_exps_ready, n)
                nc.vector.reciprocal(scale[:, :], sum_exps[:, :]).then_inc(scale_ready, 1)
                dve.wait_ge(scale_ready, n)
                nc.vector.tensor_scalar(gate[:, :], chosen[:, :], scale[:, :], SCALING, ALU.mult, ALU.mult) \
                    .then_inc(gate_ready, 1)
                dve.wait_ge(gate_ready, n)
                if c >= 1:
                    dve.wait_ge(lowT_done, n - 1)
                nc.vector.tensor_tensor(low[:, :].rearrange("p (e r) -> p e r", r=RANK),
                                        acc[:, c % 2, 2, RANKS[0]:RANKS[1]].rearrange("p (e r) -> p e r", r=RANK),
                                        gate[:, :].unsqueeze(2).broadcast_to([P, NE, RANK]), ALU.mult) \
                    .then_inc(low_ready, 1)

            def lowT_low(j, c):
                n = 2 * j + c + 1
                dve.wait_ge(lowT_hi_ready, n)
                nc.vector.tensor_tensor(lowT_lo[:, :], mixed[:, 0, 0:P], lowT_hi[:, :].bitcast(F32), ALU.subtract) \
                    .then_inc(lowT_ready, 1)

            def finish(j, c):
                n = 2 * j + c + 1
                dve.wait_ge(lora_done, n)
                dve.wait_ge(sum_ready, n)
                wide = res[:, c % 2, 0:2 * BW].rearrange("p (b m) -> p b m", b=2)
                nc.vector.tensor_tensor(wide, acc[:, c % 2, 0:2, 0:BW], wide, ALU.add)
                tail = res[:, c % 2, 2 * BW:O]
                nc.vector.tensor_tensor(tail, acc[:, c % 2, 2, 0:TAIL], tail, ALU.add).then_inc(res_ready, 1)

            dve.wait_ge(cw_hi_ready, 1)
            nc.vector.tensor_tensor(cw_parts[:, 1, :], cw_raw[:, :], cw_parts[:, 0, :].bitcast(F32), ALU.subtract) \
                .then_inc(cw_ready, 1)
            x_low(0, 0)
            y_low(0, 0)
            for k in range(KT):
                dve.wait_ge(w_hi_ready, k + 1)
                nc.vector.tensor_tensor(w_lo[:, k, :], w_raw[:, k % STAGES, :], w_hi[:, k, :].bitcast(F32),
                                        ALU.subtract).then_inc(w_ready, 1)
                if k == 0:
                    x_low(0, 1)
            dve.wait_ge(lb_hi_ready, 1)
            nc.vector.tensor_tensor(lb_lo[:, :], lb_raw[:, :], lb_hi[:, :].bitcast(F32), ALU.subtract) \
                .then_inc(lb_ready, 1)
            dve.wait_ge(consts_ready, 1)

            def step(j, c, first=False, last=0):
                if not first:
                    gating(j, c - 1)
                    lowT_low(j, c - 1)
                if last < 2:
                    y_low(j, c + 1)
                if not first:
                    finish(j, c - 1)
                if last < 1:
                    x_low(j, c + 2)

            step(0, 0, first=True)
            step(0, 1)
            with dve.Fori(0, LOOPS) as j:
                for u in (2, 3):
                    step(j, u)
            step(0, PAIRS - 2, last=1)
            step(0, PAIRS - 1, last=2)
            gating(0, PAIRS - 1)
            lowT_low(0, PAIRS - 1)
            finish(0, PAIRS - 1)

        @block.tensor
        def _(pe):
            def project(c, k):
                for part, stationary in ((0, y_hi), (1, y_lo)):
                    for b, (lo, hi) in enumerate(BANKS):
                        for moving in (w_hi, w_lo)[:2 - part]:
                            last = nc.tensor.matmul(acc[:, c % 2, b, 0:hi - lo], stationary[:, c % 2, k, :],
                                                    moving[:, k, lo:hi],
                                                    start=(k == 0 and part == 0 and moving is w_hi),
                                                    stop=(k == KT - 1 and part == 1))
                return last

            def mix(j, c, h):
                pair = 2 * j + c
                if h == 0:
                    pe.wait_ge(x_split, pair + 1)
                    pe.wait_ge(sel_ready, pair + 1)
                for k in range(HALF_K):
                    t = (h * HALF_K + k) * P
                    for b in range(2):
                        for part in range(2):
                            last = nc.tensor.matmul(mixed[:, h, k * P + b * CH:k * P + (b + 1) * CH],
                                                    x_parts[:, c % 2, b, t:t + P], w_sel[:, c % 2, b, part, :],
                                                    start=(part == 0), stop=(part == 1))
                last.then_inc(mix_done, 1)

            def transpose_low(j, c):
                pe.wait_ge(low_ready, 2 * j + c + 1)
                nc.tensor.transpose(mixed[:, 0, 0:P], low[:, :], ident[:, :]).then_inc(lowT_done, 1)

            def experts(j, c):
                pe.wait_ge(lowT_ready, 2 * j + c + 1)
                for part, stationary in ((0, lowT_hi), (1, lowT_lo)):
                    for b, (lo, hi) in enumerate(BANKS):
                        hi = min(hi, O)
                        for moving in (lb_hi, lb_lo)[:2 - part]:
                            last = nc.tensor.matmul(acc[:, c % 2, b, 0:hi - lo], stationary[:, :], moving[:, lo:hi],
                                                    start=False, stop=(part == 1), skip_group_check=True)
                last.then_inc(lora_done, 1)

            def step(j, c, first=False, last=False):
                s = 2 * j + c
                if c >= 2:
                    pe.wait_ge(res_ready, s - 1)
                for k in range(KT):
                    if k % HALF_K == 0:
                        pe.wait_ge(y_ready, 2 * s + k // HALF_K + 1)
                    if first:
                        pe.wait_ge(w_ready, k + 1)
                    done = project(c, k)
                    if k == KT - 1:
                        done.then_inc(proj_done, 1)
                    if k == 2 and not first:
                        transpose_low(j, c - 1)
                    if k == 3 and not last:
                        if not first:
                            pe.wait_ge(lowT_ready, s)
                        mix(j, c + 1, 0)
                    if k == 4 and not last:
                        mix(j, c + 1, 1)
                    if k == 5 and not first:
                        experts(j, c - 1)

            pe.wait_ge(consts_ready, 1)
            mix(0, 0, 0)
            mix(0, 0, 1)
            step(0, 0, first=True)
            pe.wait_ge(lb_ready, 1)
            step(0, 1)
            with pe.Fori(0, LOOPS) as j:
                for u in (2, 3):
                    step(j, u)
            step(0, PAIRS - 2)
            step(0, PAIRS - 1, last=True)
            transpose_low(0, PAIRS - 1)
            experts(0, PAIRS - 1)


def kernel(**inputs):
    import numpy as np
    import concourse.bacc as bacc
    from concourse.bass_utils import run_bass_kernel_spmd

    x = np.ascontiguousarray(inputs["x"])
    lora_a = np.asarray(inputs["L0_ffn_lora_A"])
    E, R, T = lora_a.shape
    base_w = np.asarray(inputs["L0_ffn_base_w"])
    cond_w = np.asarray(inputs["L0_cond_weights"])
    arrays = {
        "x": x,
        "condition": np.ascontiguousarray(inputs["itok_B_0_15"]).reshape(1, -1),
        "cond_w": np.ascontiguousarray(cond_w.transpose(1, 0, 2)).reshape(cond_w.shape[1], -1),
        "proj_w": np.ascontiguousarray(np.concatenate(
            [base_w, lora_a.reshape(E * R, T), np.asarray(inputs["L0_ffn_gate_w"])]).T),
        "lora_b": np.ascontiguousarray(np.asarray(inputs["L0_ffn_lora_B"]).transpose(0, 2, 1)).reshape(E * R, -1),
        "base_b": np.ascontiguousarray(inputs["L0_ffn_base_b"]),
    }
    nc = bacc.Bacc("TRN2", target_bir_lowering=False, num_devices=1)
    args = [nc.dram_tensor(f"in_{name}", a.shape, mybir.dt.from_np(a.dtype), kind="ExternalInput").ap()
            for name, a in arrays.items()]
    shape = (x.shape[0], x.shape[1], base_w.shape[0])
    out = nc.dram_tensor("out", shape, mybir.dt.float32, kind="ExternalOutput").ap()
    adaln_ffn_kernel(nc, *args, out)
    r = run_bass_kernel_spmd(nc, [{f"in_{name}": a for name, a in arrays.items()}], core_ids=[0])
    return r.results[0]["out"]
```

```python
from contextlib import ExitStack

import concourse.bass as bass
from concourse import mybir

ALU = mybir.AluOpType
ACT = mybir.ActivationFunctionType
F32 = mybir.dt.float32
F32R = mybir.dt.float32r
I32 = mybir.dt.int32
U32 = mybir.dt.uint32

AX_X = mybir.AxisListType.X

P = 128
TOP_K = 2
SCALING = 32.0 / 16.0


def adaln_ffn_kernel(
    nc: bass.Bass,
    x: bass.AP,
    condition: bass.AP,
    cond_w: bass.AP,
    proj_w: bass.AP,
    lora_b: bass.AP,
    base_b: bass.AP,
    out: bass.AP,
):
    B, CH, T = x.shape
    O = out.shape[2]
    ER = lora_b.shape[0]
    N = proj_w.shape[1]
    NE = N - O - ER
    RANK = ER // NE
    KT = T // P
    CONDITIONS = cond_w.shape[1] // CH
    PAIRS = B * CH // P
    HALF_K = KT // 2
    assert 2 * CH == P and ER == P and KT % 2 == 0 and PAIRS % 2 == 0 and O % 8 == 0

    BW = (N + 2) // 3 + (N + 2) // 3 % 2
    BANKS = [(0, BW), (BW, 2 * BW), (2 * BW, N)]
    TAIL = O - 2 * BW
    RANKS = (TAIL, TAIL + ER)
    GATES = (TAIL + ER, TAIL + ER + NE)
    STAGES = 4

    x_pairs = x.rearrange("(n two) c t -> n (two c) t", two=2)
    out_pairs = out.rearrange("(n two) c o -> n (two c) o", two=2)

    with ExitStack() as ctx:
        def sb(name, shape, dt):
            return ctx.enter_context(nc.sbuf_tensor(name, shape, dt))

        def sem(name):
            return ctx.enter_context(nc.semaphore(name))

        w_raw = sb("w_raw", [P, STAGES, N], F32)
        w_hi = sb("w_hi", [P, KT, N], F32R)
        w_lo = sb("w_lo", [P, KT, N], F32R)
        lb_raw = sb("lb_raw", [P, O], F32)
        lb_hi = sb("lb_hi", [P, O], F32R)
        lb_lo = sb("lb_lo", [P, O], F32R)
        bias = sb("bias", [P, O], F32)
        cw = sb("cw", [P, cond_w.shape[1]], F32)
        cond_sb = sb("cond_sb", [1, B], I32)
        ident = sb("ident", [P, P], F32)
        earlier = sb("earlier", [P, NE, NE], F32)

        x_sb = sb("x_sb", [P, 2, T], F32)
        w_pair = sb("w_pair", [P, 2, P], F32)
        y_hi = sb("y_hi", [P, 2, KT, P], F32R)
        y_lo = sb("y_lo", [P, 2, KT, P], F32R)
        res = sb("res", [P, 2, O], F32)
        logits_sb = sb("logits_sb", [P, NE], F32)
        top = sb("top", [P, 1], F32)
        below = sb("below", [P, NE], F32)
        exps = sb("exps", [P, NE], F32)
        greater = sb("greater", [P, NE, NE], F32)
        ties = sb("ties", [P, NE, NE], F32)
        rank = sb("rank", [P, NE], F32)
        chosen = sb("chosen", [P, NE], F32)
        sum_exps = sb("sum_exps", [P, 1], F32)
        scale = sb("scale", [P, 1], F32)
        gate = sb("gate", [P, NE], F32)
        low = sb("low", [P, ER], F32)
        lowT_hi = sb("lowT_hi", [P, P], F32R)
        lowT_lo = sb("lowT_lo", [P, P], F32R)

        acc = ctx.enter_context(nc.psum_tensor("acc", [P, 2, 3, 512], F32))
        mixed = ctx.enter_context(nc.psum_tensor("mixed", [P, 2, 512], F32))

        cond_in = sem("cond_in")
        cw_in = sem("cw_in")
        w_in = [sem(f"w_in{i}") for i in range(STAGES)]
        lb_in = sem("lb_in")
        bias_in = sem("bias_in")
        w_hi_ready = sem("w_hi_ready")
        w_ready = sem("w_ready")
        lb_hi_ready = sem("lb_hi_ready")
        lb_ready = sem("lb_ready")
        w_pair_zero = sem("w_pair_zero")
        ident_zero = sem("ident_zero")
        consts_ready = sem("consts_ready")
        x_in = [sem("x_in0"), sem("x_in1")]
        stored = [sem("stored0"), sem("stored1")]
        sel_ready = sem("sel_ready")
        mix_done = sem("mix_done")
        y_hi_ready = sem("y_hi_ready")
        y_ready = sem("y_ready")
        proj_done = sem("proj_done")
        logits_ready = sem("logits_ready")
        top_ready = sem("top_ready")
        below_ready = sem("below_ready")
        exp_ready = sem("exp_ready")
        compared = sem("compared")
        ties_ready = sem("ties_ready")
        ahead_ready = sem("ahead_ready")
        rank_ready = sem("rank_ready")
        chosen_ready = sem("chosen_ready")
        sum_exps_ready = sem("sum_exps_ready")
        scale_ready = sem("scale_ready")
        gate_ready = sem("gate_ready")
        low_ready = sem("low_ready")
        lowT_done = sem("lowT_done")
        lowT_hi_ready = sem("lowT_hi_ready")
        lowT_ready = sem("lowT_ready")
        lora_done = sem("lora_done")
        sum_ready = sem("sum_ready")
        res_ready = sem("res_ready")

        block = ctx.enter_context(nc.Block())

        LOOPS = (PAIRS - 4) // 2

        @block.sync
        def _(sp):
            sp.dma_start(cond_sb[:, :], condition).then_inc(cond_in, 16)
            for half in range(2):
                sp.dma_start(cw[half * CH:(half + 1) * CH, :], cond_w).then_inc(cw_in, 16)

            def load_x(j, c):
                sp.dma_start(x_sb[:, c % 2, :], x_pairs[2 * j + c]).then_inc(x_in[c % 2], 16)

            load_x(0, 0)
            for k in range(KT):
                if k >= STAGES:
                    sp.wait_ge(w_hi_ready, k - STAGES + 1)
                    sp.wait_ge(w_ready, k - STAGES + 1)
                sp.dma_start(w_raw[:, k % STAGES, :], proj_w[k * P:(k + 1) * P, :]).then_inc(w_in[k % STAGES], 16)
                if k == 0:
                    load_x(0, 1)
            sp.dma_start(bias[:, :], base_b.partition_broadcast(P)).then_inc(bias_in, 16)
            sp.dma_start(lb_raw[:, :], lora_b).then_inc(lb_in, 16)

            def step(j, c, first=False, last=False):
                s = 2 * j + c
                if not last:
                    mixed_halves = 2 * s + 2 if type(j) is int else sp.snap(2 * s + 2)
                    sp.wait_ge(sum_ready, s + 1)
                    sp.wait_ge(mix_done, mixed_halves)
                    load_x(j, c + 2)
                if not first:
                    store(j, c - 1)

            def store(j, c):
                sp.wait_ge(res_ready, 2 * j + c + 1)
                sp.dma_start(out_pairs[2 * j + c], res[:, c % 2, :]).then_inc(stored[c % 2], 16)

            step(0, 0, first=True)
            step(0, 1)
            with sp.Fori(0, LOOPS) as j:
                for u in (2, 3):
                    step(j, u)
            for s in (PAIRS - 2, PAIRS - 1):
                step(0, s, last=True)
            store(0, PAIRS - 1)
            for i in range(2):
                sp.wait_ge(stored[i], 16 * (PAIRS // 2))

        @block.gpsimd
        def _(pool):
            nc.gpsimd.memset(w_pair[:, :, :], 0.0).then_inc(w_pair_zero, 1)
            nc.gpsimd.memset(ident[:, :], 0.0).then_inc(ident_zero, 1)
            nc.gpsimd.memset(earlier[:, :, :], 0.0).then_inc(ident_zero, 1)
            pool.wait_ge(ident_zero, 2)
            for e in range(1, NE):
                nc.gpsimd.memset(earlier[:, e, 0:e], 1.0).then_inc(consts_ready, 1)
            nc.gpsimd.affine_select(out=ident[:, :], in_=ident[:, :], compare_op=ALU.not_equal, fill=1.0, base=0,
                                    pattern=[[-1, P]], channel_multiplier=1).then_inc(consts_ready, 1)

            def select(j, c):
                if c >= 2:
                    pool.wait_ge(mix_done, 2 * (2 * j + c) - 2)
                pool.wait_ge(sum_ready, 2 * j + c - 1) if c >= 2 else pool.wait_ge(consts_ready, NE)
                for b in range(2):
                    if b == 1 or c == 1:
                        pool.wait_ge(sel_ready, 2 * (2 * j + c) + b)
                    half = slice(b * CH, (b + 1) * CH)
                    cond = pool.value_load(cond_sb[0:1, bass.ds(4 * j + 2 * c + b, 1)], min_val=0,
                                           max_val=CONDITIONS - 1)
                    nc.gpsimd.tensor_copy(w_pair[half, c % 2, half], cw[half, bass.ds(cond * CH, CH)]) \
                        .then_inc(sel_ready, 1)

            def add_bias(j, c):
                if c >= 2:
                    pool.wait_ge(stored[c % 2], 16 * (j + c // 2))
                pool.wait_ge(x_in[c % 2], 16 * (j + c // 2 + 1))
                pool.wait_ge(sel_ready, 2 * min(PAIRS, 2 * j + c + 2) if type(j) is int else 2 * (2 * j + c + 2))
                nc.gpsimd.tensor_tensor(res[:, c % 2, :], x_sb[:, c % 2, :], bias[:, :], ALU.add).then_inc(sum_ready, 1)

            pool.wait_ge(cond_in, 16)
            pool.wait_ge(cw_in, 32)
            pool.wait_ge(w_pair_zero, 1)
            select(0, 0)
            select(0, 1)
            pool.wait_ge(bias_in, 16)
            add_bias(0, 0)
            select(0, 2)
            add_bias(0, 1)
            select(0, 3)
            with pool.Fori(0, LOOPS) as j:
                for u in (2, 3):
                    add_bias(j, u)
                    select(j, u + 2)
            add_bias(0, PAIRS - 2)
            add_bias(0, PAIRS - 1)

        @block.scalar
        def _(act):
            def y_high(j, c):
                if c >= 2:
                    act.wait_ge(proj_done, 2 * j + c - 1)
                for h in range(2):
                    act.wait_ge(mix_done, 2 * (2 * j + c) + h + 1)
                    nc.scalar.copy(y_hi[:, c % 2, h * HALF_K:(h + 1) * HALF_K, :],
                                   mixed[:, h, :].rearrange("p (k m) -> p k m", m=P)).then_inc(y_hi_ready, 1)

            def gate_exp(j, c):
                act.wait_ge(below_ready, 2 * j + c + 1)
                nc.scalar.activation(exps[:, :], below[:, :], ACT.Exp).then_inc(exp_ready, 1)

            def lowT_high(j, c):
                act.wait_ge(lowT_done, 2 * j + c + 1)
                if c >= 1:
                    act.wait_ge(lora_done, 2 * j + c)
                nc.scalar.copy(lowT_hi[:, :], mixed[:, 0, 0:P]).then_inc(lowT_hi_ready, 1)

            y_high(0, 0)
            for k in range(KT):
                act.wait_ge(w_in[k % STAGES], 16 * (k // STAGES + 1))
                nc.scalar.copy(w_hi[:, k, :], w_raw[:, k % STAGES, :]).then_inc(w_hi_ready, 1)
            act.wait_ge(lb_in, 16)
            nc.scalar.copy(lb_hi[:, :], lb_raw[:, :]).then_inc(lb_hi_ready, 1)

            def step(j, c, first=False, last=False):
                if not first:
                    gate_exp(j, c - 1)
                    lowT_high(j, c - 1)
                if not last:
                    y_high(j, c + 1)

            step(0, 0, first=True)
            step(0, 1)
            with act.Fori(0, LOOPS) as j:
                for u in (2, 3):
                    step(j, u)
            step(0, PAIRS - 2)
            step(0, PAIRS - 1, last=True)
            gate_exp(0, PAIRS - 1)
            lowT_high(0, PAIRS - 1)

        @block.vector
        def _(dve):
            def y_low(j, c):
                for h in range(2):
                    dve.wait_ge(y_hi_ready, 2 * (2 * j + c) + h + 1)
                    ks = slice(h * HALF_K, (h + 1) * HALF_K)
                    nc.vector.tensor_tensor(y_lo[:, c % 2, ks, :], mixed[:, h, :].rearrange("p (k m) -> p k m", m=P),
                                            y_hi[:, c % 2, ks, :].bitcast(F32), ALU.subtract).then_inc(y_ready, 1)

            def gating(j, c):
                n = 2 * j + c + 1
                logits = logits_sb[:, :]
                here = logits.unsqueeze(2).broadcast_to([P, NE, NE])
                other = logits.unsqueeze(1).broadcast_to([P, NE, NE])
                dve.wait_ge(proj_done, n)
                nc.vector.tensor_copy(logits_sb[:, :], acc[:, c % 2, 2, GATES[0]:GATES[1]]).then_inc(logits_ready, 1)
                dve.wait_ge(logits_ready, n)
                nc.vector.reduce_max(top[:, :], logits, AX_X).then_inc(top_ready, 1)
                nc.vector.tensor_tensor(ties[:, :, :], other, here, ALU.is_equal).then_inc(compared, 1)
                dve.wait_ge(top_ready, n)
                nc.vector.tensor_scalar(below[:, :], logits, top[:, :], None, ALU.subtract).then_inc(below_ready, 1)
                nc.vector.tensor_tensor(greater[:, :, :], other, here, ALU.is_gt).then_inc(compared, 1)
                dve.wait_ge(compared, 2 * n)
                nc.vector.tensor_tensor(ties[:, :, :], ties[:, :, :], earlier[:, :, :], ALU.mult) \
                    .then_inc(ties_ready, 1)
                dve.wait_ge(ties_ready, n)
                nc.vector.tensor_tensor(greater[:, :, :], greater[:, :, :], ties[:, :, :], ALU.add) \
                    .then_inc(ahead_ready, 1)
                dve.wait_ge(ahead_ready, n)
                nc.vector.reduce_sum(rank[:, :], greater[:, :, :], AX_X).then_inc(rank_ready, 1)
                dve.wait_ge(rank_ready, n)
                dve.wait_ge(exp_ready, n)
                nc.vector.scalar_tensor_tensor(out=chosen[:, :], in0=rank[:, :], scalar=float(TOP_K), in1=exps[:, :],
                                               op0=ALU.is_lt, op1=ALU.mult).then_inc(chosen_ready, 1)
                dve.wait_ge(chosen_ready, n)
                nc.vector.reduce_sum(sum_exps[:, :], chosen[:, :], AX_X).then_inc(sum_exps_ready, 1)
                dve.wait_ge(sum_exps_ready, n)
                nc.vector.reciprocal(scale[:, :], sum_exps[:, :]).then_inc(scale_ready, 1)
                dve.wait_ge(scale_ready, n)
                nc.vector.tensor_scalar(gate[:, :], chosen[:, :], scale[:, :], SCALING, ALU.mult, ALU.mult) \
                    .then_inc(gate_ready, 1)
                dve.wait_ge(gate_ready, n)
                if c >= 1:
                    dve.wait_ge(lowT_done, n - 1)
                nc.vector.tensor_tensor(low[:, :].rearrange("p (e r) -> p e r", r=RANK),
                                        acc[:, c % 2, 2, RANKS[0]:RANKS[1]].rearrange("p (e r) -> p e r", r=RANK),
                                        gate[:, :].unsqueeze(2).broadcast_to([P, NE, RANK]), ALU.mult) \
                    .then_inc(low_ready, 1)

            def lowT_low(j, c):
                n = 2 * j + c + 1
                dve.wait_ge(lowT_hi_ready, n)
                nc.vector.tensor_tensor(lowT_lo[:, :], mixed[:, 0, 0:P], lowT_hi[:, :].bitcast(F32), ALU.subtract) \
                    .then_inc(lowT_ready, 1)

            def finish(j, c):
                n = 2 * j + c + 1
                dve.wait_ge(lora_done, n)
                dve.wait_ge(sum_ready, n)
                wide = res[:, c % 2, 0:2 * BW].rearrange("p (b m) -> p b m", b=2)
                nc.vector.tensor_tensor(wide, acc[:, c % 2, 0:2, 0:BW], wide, ALU.add)
                tail = res[:, c % 2, 2 * BW:O]
                nc.vector.tensor_tensor(tail, acc[:, c % 2, 2, 0:TAIL], tail, ALU.add).then_inc(res_ready, 1)

            y_low(0, 0)
            for k in range(KT):
                dve.wait_ge(w_hi_ready, k + 1)
                nc.vector.tensor_tensor(w_lo[:, k, :], w_raw[:, k % STAGES, :], w_hi[:, k, :].bitcast(F32),
                                        ALU.subtract).then_inc(w_ready, 1)
            dve.wait_ge(lb_hi_ready, 1)
            nc.vector.tensor_tensor(lb_lo[:, :], lb_raw[:, :], lb_hi[:, :].bitcast(F32), ALU.subtract) \
                .then_inc(lb_ready, 1)
            dve.wait_ge(consts_ready, NE)

            def step(j, c, first=False, last=False):
                if not first:
                    gating(j, c - 1)
                    lowT_low(j, c - 1)
                if not last:
                    y_low(j, c + 1)
                if not first:
                    finish(j, c - 1)

            step(0, 0, first=True)
            step(0, 1)
            with dve.Fori(0, LOOPS) as j:
                for u in (2, 3):
                    step(j, u)
            step(0, PAIRS - 2)
            step(0, PAIRS - 1, last=True)
            gating(0, PAIRS - 1)
            lowT_low(0, PAIRS - 1)
            finish(0, PAIRS - 1)

        @block.tensor
        def _(pe):
            def project(c, k):
                for part, stationary in ((0, y_hi), (1, y_lo)):
                    for b, (lo, hi) in enumerate(BANKS):
                        for moving in (w_hi, w_lo)[:2 - part]:
                            last = nc.tensor.matmul(acc[:, c % 2, b, 0:hi - lo], stationary[:, c % 2, k, :],
                                                    moving[:, k, lo:hi],
                                                    start=(k == 0 and part == 0 and moving is w_hi),
                                                    stop=(k == KT - 1 and part == 1))
                return last

            def mix(j, c, h):
                pair = 2 * j + c
                if h == 0:
                    pe.wait_ge(x_in[c % 2], 16 * (j + c // 2 + 1))
                    pe.wait_ge(sel_ready, 2 * pair + 2)
                for k in range(HALF_K):
                    t = (h * HALF_K + k) * P
                    last = nc.tensor.matmul(mixed[:, h, k * P:(k + 1) * P], x_sb[:, c % 2, t:t + P],
                                            w_pair[:, c % 2, :], start=True, stop=True)
                last.then_inc(mix_done, 1)

            def transpose_low(j, c):
                pe.wait_ge(low_ready, 2 * j + c + 1)
                nc.tensor.transpose(mixed[:, 0, 0:P], low[:, :], ident[:, :]).then_inc(lowT_done, 1)

            def experts(j, c):
                pe.wait_ge(lowT_ready, 2 * j + c + 1)
                for part, stationary in ((0, lowT_hi), (1, lowT_lo)):
                    for b, (lo, hi) in enumerate(BANKS):
                        hi = min(hi, O)
                        for moving in (lb_hi, lb_lo)[:2 - part]:
                            last = nc.tensor.matmul(acc[:, c % 2, b, 0:hi - lo], stationary[:, :], moving[:, lo:hi],
                                                    start=False, stop=(part == 1), skip_group_check=True)
                last.then_inc(lora_done, 1)

            def step(j, c, first=False, last=False):
                s = 2 * j + c
                if c >= 2:
                    pe.wait_ge(res_ready, s - 1)
                for k in range(KT):
                    if k % HALF_K == 0:
                        pe.wait_ge(y_ready, 2 * s + k // HALF_K + 1)
                    if first:
                        pe.wait_ge(w_ready, k + 1)
                    done = project(c, k)
                    if k == KT - 1:
                        done.then_inc(proj_done, 1)
                    if k == 2 and not first:
                        transpose_low(j, c - 1)
                    if k == 3 and not last:
                        if not first:
                            pe.wait_ge(lowT_ready, s)
                        mix(j, c + 1, 0)
                    if k == 4 and not last:
                        mix(j, c + 1, 1)
                    if k == 5 and not first:
                        experts(j, c - 1)

            pe.wait_ge(consts_ready, NE)
            mix(0, 0, 0)
            mix(0, 0, 1)
            step(0, 0, first=True)
            pe.wait_ge(lb_ready, 1)
            step(0, 1)
            with pe.Fori(0, LOOPS) as j:
                for u in (2, 3):
                    step(j, u)
            step(0, PAIRS - 2)
            step(0, PAIRS - 1, last=True)
            transpose_low(0, PAIRS - 1)
            experts(0, PAIRS - 1)


def kernel(**inputs):
    import numpy as np
    import concourse.bacc as bacc
    from concourse.bass_utils import run_bass_kernel_spmd

    x = np.ascontiguousarray(inputs["x"])
    lora_a = np.asarray(inputs["L0_ffn_lora_A"])
    E, R, T = lora_a.shape
    base_w = np.asarray(inputs["L0_ffn_base_w"])
    cond_w = np.asarray(inputs["L0_cond_weights"])
    arrays = {
        "x": x,
        "condition": np.ascontiguousarray(inputs["itok_B_0_15"]).reshape(1, -1),
        "cond_w": np.ascontiguousarray(cond_w.transpose(1, 0, 2)).reshape(cond_w.shape[1], -1),
        "proj_w": np.ascontiguousarray(np.concatenate(
            [base_w, lora_a.reshape(E * R, T), np.asarray(inputs["L0_ffn_gate_w"])]).T),
        "lora_b": np.ascontiguousarray(np.asarray(inputs["L0_ffn_lora_B"]).transpose(0, 2, 1)).reshape(E * R, -1),
        "base_b": np.ascontiguousarray(inputs["L0_ffn_base_b"]),
    }
    nc = bacc.Bacc("TRN2", target_bir_lowering=False, num_devices=1)
    args = [nc.dram_tensor(f"in_{name}", a.shape, mybir.dt.from_np(a.dtype), kind="ExternalInput").ap()
            for name, a in arrays.items()]
    shape = (x.shape[0], x.shape[1], base_w.shape[0])
    out = nc.dram_tensor("out", shape, mybir.dt.float32, kind="ExternalOutput").ap()
    adaln_ffn_kernel(nc, *args, out)
    r = run_bass_kernel_spmd(nc, [{f"in_{name}": a for name, a in arrays.items()}], core_ids=[0])
    return r.results[0]["out"]
```

```python
from contextlib import ExitStack

import concourse.bass as bass
from concourse import mybir

ALU = mybir.AluOpType
ACT = mybir.ActivationFunctionType
F32 = mybir.dt.float32
F32R = mybir.dt.float32r
I32 = mybir.dt.int32
AX_X = mybir.AxisListType.X

P = 128
TOP_K = 2
SCALING = 32.0 / 16.0


def adaln_ffn_kernel(
    nc: bass.Bass,
    x: bass.AP,
    condition: bass.AP,
    cond_w: bass.AP,
    proj_w: bass.AP,
    lora_b: bass.AP,
    base_b: bass.AP,
    out: bass.AP,
):
    B, CH, T = x.shape
    O = out.shape[2]
    ER = lora_b.shape[0]
    N = proj_w.shape[1]
    NE = N - O - ER
    RANK = ER // NE
    KT = T // P
    CONDITIONS = cond_w.shape[1] // CH
    PAIRS = B * CH // P
    HALF_K = KT // 2
    SQ = 32
    QUARTERS = P // SQ
    TQ = T // QUARTERS
    assert 2 * CH == P and ER == P and T == 2 * 512 and PAIRS % 4 == 0 and O % 8 == 0

    BW = (N + 2) // 3 + (N + 2) // 3 % 2
    BANKS = [(0, BW), (BW, 2 * BW), (2 * BW, N)]
    TAIL = O - 2 * BW
    RANKS = (TAIL, TAIL + ER)
    GATES = (TAIL + ER, TAIL + ER + NE)
    STAGES = 4

    x_pairs = x.rearrange("(n two) c t -> n (two c) t", two=2)
    w_blocks = proj_w.rearrange("(p k) n -> k p n", k=KT)
    out_pairs = out.rearrange("(n two) c o -> n (two c) o", two=2)

    with ExitStack() as ctx:
        def sb(name, shape, dt):
            return ctx.enter_context(nc.sbuf_tensor(name, shape, dt))

        def sem(name):
            return ctx.enter_context(nc.semaphore(name))

        w_raw = sb("w_raw", [P, STAGES, N], F32)
        w_hi = sb("w_hi", [P, KT, N], F32R)
        w_lo = sb("w_lo", [P, KT, N], F32R)
        lb_raw = sb("lb_raw", [P, O], F32)
        lb_hi = sb("lb_hi", [P, O], F32R)
        lb_lo = sb("lb_lo", [P, O], F32R)
        bias = sb("bias", [P, O], F32)
        cw = sb("cw", [P, cond_w.shape[1]], F32)
        cw_parts = sb("cw_parts", [P, 2, cond_w.shape[1]], F32R)
        cond_sb = sb("cond_sb", [1, B], I32)
        ident = sb("ident", [P, P], F32)
        earlier = sb("earlier", [P, NE, NE], F32)

        x_sb = sb("x_sb", [P, 4, T], F32)
        x_parts = sb("x_parts", [P, 2, T], F32R)
        w_pair = sb("w_pair", [P, 2, P], F32)
        w_sel = sb("w_sel", [P, 2, 2, P], F32R)
        y_moved = sb("y_moved", [P, QUARTERS, TQ], F32)
        y_turned = sb("y_turned", [P, QUARTERS, KT, SQ], F32)
        y_hi = sb("y_hi", [P, 2, KT, P], F32R)
        y_lo = sb("y_lo", [P, 2, KT, P], F32R)
        res = sb("res", [P, 4, O], F32)
        logits_sb = sb("logits_sb", [P, NE], F32)
        top = sb("top", [P, 1], F32)
        below = sb("below", [P, NE], F32)
        exps = sb("exps", [P, NE], F32)
        greater = sb("greater", [P, NE, NE], F32)
        ties = sb("ties", [P, NE, NE], F32)
        rank = sb("rank", [P, NE], F32)
        chosen = sb("chosen", [P, NE], F32)
        sum_exps = sb("sum_exps", [P, 1], F32)
        scale = sb("scale", [P, 1], F32)
        gate = sb("gate", [P, NE], F32)
        low = sb("low", [P, ER], F32)
        lowT_hi = sb("lowT_hi", [P, P], F32R)
        lowT_lo = sb("lowT_lo", [P, P], F32R)

        acc = ctx.enter_context(nc.psum_tensor("acc", [P, 2, 3, 512], F32))
        mixed = ctx.enter_context(nc.psum_tensor("mixed", [P, 2, 512], F32))

        cond_in = sem("cond_in")
        cw_in = sem("cw_in")
        w_in = [sem(f"w_in{i}") for i in range(STAGES)]
        lb_in = sem("lb_in")
        bias_in = sem("bias_in")
        w_hi_ready = sem("w_hi_ready")
        w_ready = sem("w_ready")
        lb_hi_ready = sem("lb_hi_ready")
        lb_ready = sem("lb_ready")
        w_zero = sem("w_zero")
        cw_hi_ready = sem("cw_hi_ready")
        cw_ready = sem("cw_ready")
        ident_zero = sem("ident_zero")
        consts_ready = sem("consts_ready")
        x_in = [sem(f"x_in{i}") for i in range(4)]
        stored = [sem(f"stored{i}") for i in range(4)]
        x_hi_ready = sem("x_hi_ready")
        x_split = sem("x_split")
        moved = sem("moved")
        turned = sem("turned")
        sel_ready = sem("sel_ready")
        mix_done = sem("mix_done")
        y_hi_ready = sem("y_hi_ready")
        y_ready = sem("y_ready")
        proj_done = sem("proj_done")
        logits_ready = sem("logits_ready")
        top_ready = sem("top_ready")
        below_ready = sem("below_ready")
        exp_ready = sem("exp_ready")
        compared = sem("compared")
        ties_ready = sem("ties_ready")
        ahead_ready = sem("ahead_ready")
        rank_ready = sem("rank_ready")
        chosen_ready = sem("chosen_ready")
        sum_exps_ready = sem("sum_exps_ready")
        scale_ready = sem("scale_ready")
        gate_ready = sem("gate_ready")
        low_ready = sem("low_ready")
        lowT_done = sem("lowT_done")
        lowT_hi_ready = sem("lowT_hi_ready")
        lowT_ready = sem("lowT_ready")
        lora_done = sem("lora_done")
        sum_ready = sem("sum_ready")
        res_ready = sem("res_ready")

        def turned_half(h):
            return y_turned[:, :, h * HALF_K:(h + 1) * HALF_K, :].rearrange("p g k m -> p k g m")

        block = ctx.enter_context(nc.Block())

        LOOPS = (PAIRS - 4) // 4

        @block.sync
        def _(sp):
            sp.dma_start(cond_sb[:, :], condition).then_inc(cond_in, 16)
            for half in range(2):
                sp.dma_start(cw[half * CH:(half + 1) * CH, :], cond_w).then_inc(cw_in, 16)

            def load_x(j, c):
                sp.dma_start(x_sb[:, c % 4, :], x_pairs[4 * j + c]).then_inc(x_in[c % 4], 16)

            load_x(0, 0)
            for k in range(KT):
                if k >= STAGES:
                    sp.wait_ge(w_hi_ready, k - STAGES + 1)
                    sp.wait_ge(w_ready, k - STAGES + 1)
                sp.dma_start(w_raw[:, k % STAGES, :], w_blocks[k]).then_inc(w_in[k % STAGES], 16)
                if k == 3:
                    load_x(0, 1)
            load_x(0, 2)
            sp.dma_start(bias[:, :], base_b.partition_broadcast(P)).then_inc(bias_in, 16)
            sp.dma_start(lb_raw[:, :], lora_b).then_inc(lb_in, 16)
            load_x(0, 3)

            def store(j, c):
                sp.wait_ge(res_ready, 4 * j + c + 1)
                sp.dma_start(out_pairs[4 * j + c], res[:, c % 4, :]).then_inc(stored[c % 4], 16)

            with sp.Fori(0, LOOPS) as j:
                for u in range(4):
                    sp.wait_ge(sum_ready, 4 * j + u + 3)
                    load_x(j, u + 4)
                    store(j, u)
            for n in range(PAIRS - 4, PAIRS - 1):
                store(0, n)
            last = PAIRS - 1
            sp.wait_ge(res_ready, PAIRS)
            sp.dma_start(out_pairs[last, :, 0:BW], res[:, last % 4, 0:BW]).then_inc(stored[last % 4], 16)
            sp.dma_start(out_pairs[last, :, 2 * BW:O], res[:, last % 4, 2 * BW:O]).then_inc(stored[last % 4], 16)
            sp.wait_ge(res_ready, PAIRS + 1)
            sp.dma_start(out_pairs[last, :, BW:2 * BW], res[:, last % 4, BW:2 * BW]).then_inc(stored[last % 4], 16)
            for i in range(4):
                sp.wait_ge(stored[i], 16 * (PAIRS // 4 + (2 if i == last % 4 else 0)))

        @block.gpsimd
        def _(pool):
            nc.gpsimd.memset(w_pair[:, :, :], 0.0).then_inc(w_zero, 1)
            nc.gpsimd.memset(w_sel[:, :, :, :].bitcast(F32), 0.0).then_inc(w_zero, 1)
            nc.gpsimd.memset(ident[:, :], 0.0).then_inc(ident_zero, 1)
            nc.gpsimd.memset(earlier[:, :, :], 0.0).then_inc(ident_zero, 1)
            pool.wait_ge(ident_zero, 2)
            for e in range(1, NE):
                nc.gpsimd.memset(earlier[:, e, 0:e], 1.0).then_inc(consts_ready, 1)
            nc.gpsimd.affine_select(out=ident[:, :], in_=ident[:, :], compare_op=ALU.not_equal, fill=1.0, base=0,
                                    pattern=[[-1, P]], channel_multiplier=1).then_inc(consts_ready, 1)


            def select(j, c):
                n = 4 * j + c
                whole = c < 2
                if c == 0:
                    pool.wait_ge(consts_ready, NE)
                elif c < 3:
                    pool.wait_ge(sel_ready, 2 * c)
                else:
                    pool.wait_ge(sum_ready, n)
                if c == 2:
                    pool.wait_ge(cw_ready, 1)
                if c >= 2:
                    pool.wait_ge(mix_done, 2 * n - 2)
                for b in range(2):
                    if b == 1:
                        pool.wait_ge(sel_ready, 2 * n + b)
                    half = slice(b * CH, (b + 1) * CH)
                    cond = pool.value_load(cond_sb[0:1, bass.ds(8 * j + 2 * c + b, 1)], min_val=0,
                                           max_val=CONDITIONS - 1)
                    if whole:
                        done = nc.gpsimd.tensor_copy(w_pair[half, c, half], cw[half, bass.ds(cond * CH, CH)])
                    else:
                        done = nc.gpsimd.tensor_copy(w_sel[half, c % 2, :, half],
                                                     cw_parts[half, :, bass.ds(cond * CH, CH)])
                    done.then_inc(sel_ready, 1)

            def add_bias(j, c):
                n = 4 * j + c
                if c >= 4:
                    pool.wait_ge(stored[c % 4], 16 * (j + c // 4))
                pool.wait_ge(x_in[c % 4], 16 * (j + c // 4 + 1))
                pool.wait_ge(sel_ready, 2 * n + 2 if c >= 3 else 6)
                nc.gpsimd.tensor_tensor(res[:, c % 4, :], x_sb[:, c % 4, :], bias[:, :], ALU.add).then_inc(sum_ready, 1)

            pool.wait_ge(cond_in, 16)
            pool.wait_ge(cw_in, 32)
            pool.wait_ge(w_zero, 2)
            select(0, 0)
            select(0, 1)
            pool.wait_ge(cw_hi_ready, 1)
            pool.wait_ge(sel_ready, 4)
            nc.gpsimd.tensor_tensor(cw_parts[:, 1, :], cw[:, :], cw_parts[:, 0, :].bitcast(F32), ALU.subtract) \
                .then_inc(cw_ready, 1)
            select(0, 2)
            pool.wait_ge(bias_in, 16)
            for n in range(3):
                add_bias(0, n)
            select(0, 3)
            add_bias(0, 3)
            with pool.Fori(0, LOOPS) as j:
                for u in (4, 5, 6, 7):
                    select(j, u)
                    add_bias(j, u)

        @block.scalar
        def _(act):
            def y_high(j, c, h):
                n = 4 * j + c
                if c >= 2:
                    act.wait_ge(proj_done, n - 1)
                    act.wait_ge(turned, 2 * (n - 2) + h + 1)
                    y = turned_half(h)
                else:
                    act.wait_ge(mix_done, 2 * n + h + 1)
                    y = mixed[:, h, :].rearrange("p (k m) -> p k m", m=P)
                high = y_hi[:, c % 2, h * HALF_K:(h + 1) * HALF_K, :]
                if c >= 2:
                    high = high.rearrange("p k (g m) -> p k g m", m=SQ)
                nc.scalar.copy(high, y).then_inc(y_hi_ready, 1)

            def move(j, c):
                n = 4 * j + c
                if c >= 3:
                    act.wait_ge(turned, 2 * (n - 3) + 2)
                for h in range(2):
                    act.wait_ge(mix_done, 2 * n + h + 1)
                    for q in (2 * h, 2 * h + 1):
                        for g in range(QUARTERS):
                            last = nc.scalar.copy(y_moved[q * SQ:(q + 1) * SQ, g, :],
                                                  mixed[g * SQ:(g + 1) * SQ, h, q % 2 * TQ:(q % 2 + 1) * TQ])
                    last.then_inc(moved, 1)

            def x_high(j, c):
                n = 4 * j + c
                act.wait_ge(x_in[c % 4], 16 * (j + c // 4 + 1))
                if c >= 3:
                    act.wait_ge(mix_done, 2 * n)
                nc.scalar.copy(x_parts[:, 0, :], x_sb[:, c % 4, :]).then_inc(x_hi_ready, 1)

            def gate_exp(j, c):
                act.wait_ge(below_ready, 4 * j + c + 1)
                nc.scalar.activation(exps[:, :], below[:, :], ACT.Exp).then_inc(exp_ready, 1)

            def lowT_high(j, c):
                act.wait_ge(lowT_done, 4 * j + c + 1)
                if c >= 1:
                    act.wait_ge(lora_done, 4 * j + c)
                nc.scalar.copy(lowT_hi[:, :], mixed[:, 0, 0:P]).then_inc(lowT_hi_ready, 1)

            for k in range(KT):
                if k == 0:
                    y_high(0, 0, 0)
                if k == 1:
                    y_high(0, 0, 1)
                act.wait_ge(w_in[k % STAGES], 16 * (k // STAGES + 1))
                nc.scalar.copy(w_hi[:, k, :], w_raw[:, k % STAGES, :]).then_inc(w_hi_ready, 1)
                if k == 2:
                    act.wait_ge(cw_in, 32)
                    nc.scalar.copy(cw_parts[:, 0, :], cw[:, :]).then_inc(cw_hi_ready, 1)

            y_high(0, 1, 0)
            y_high(0, 1, 1)
            x_high(0, 2)
            act.wait_ge(lb_in, 16)
            nc.scalar.copy(lb_hi[:, :], lb_raw[:, :]).then_inc(lb_hi_ready, 1)

            def step(j, c, split=True, ahead=True):
                gate_exp(j, c - 1)
                if ahead:
                    move(j, c + 1)
                lowT_high(j, c - 1)
                if ahead:
                    y_high(j, c + 1, 0)
                    y_high(j, c + 1, 1)
                if split:
                    x_high(j, c + 2)

            step(0, 1)
            with act.Fori(0, LOOPS) as j:
                for u in (2, 3, 4, 5):
                    step(j, u)
            step(0, PAIRS - 2, split=False)
            step(0, PAIRS - 1, split=False, ahead=False)
            gate_exp(0, PAIRS - 1)
            lowT_high(0, PAIRS - 1)

        @block.vector
        def _(dve):
            def y_low(j, c, h):
                dve.wait_ge(y_hi_ready, 2 * (4 * j + c) + h + 1)
                ks = slice(h * HALF_K, (h + 1) * HALF_K)
                y = turned_half(h) if c >= 2 else mixed[:, h, :].rearrange("p (k m) -> p k m", m=P)
                high = y_hi[:, c % 2, ks, :].bitcast(F32)
                low_part = y_lo[:, c % 2, ks, :]
                if c >= 2:
                    high = high.rearrange("p k (g m) -> p k g m", m=SQ)
                    low_part = low_part.rearrange("p k (g m) -> p k g m", m=SQ)
                nc.vector.tensor_tensor(low_part, y, high, ALU.subtract).then_inc(y_ready, 1)

            def turn(j, c):
                dve.wait_ge(moved, 2 * (4 * j + c - 2) + 2)
                squares = y_moved[:, :, :].rearrange("p g (a k) -> p g k a", k=KT)
                for h in range(2):
                    ks = slice(h * HALF_K, (h + 1) * HALF_K)
                    nc.vector.transpose(y_turned[:, :, ks, :], squares[:, :, ks, :]).then_inc(turned, 1)

            def x_low(j, c):
                dve.wait_ge(x_hi_ready, 4 * j + c - 1)
                nc.vector.tensor_tensor(x_parts[:, 1, :], x_sb[:, c % 4, :], x_parts[:, 0, :].bitcast(F32),
                                        ALU.subtract).then_inc(x_split, 1)

            def gating(j, c):
                n = 4 * j + c + 1
                logits = logits_sb[:, :]
                here = logits.unsqueeze(2).broadcast_to([P, NE, NE])
                other = logits.unsqueeze(1).broadcast_to([P, NE, NE])
                dve.wait_ge(proj_done, n)
                nc.vector.tensor_copy(logits_sb[:, :], acc[:, c % 2, 2, GATES[0]:GATES[1]]).then_inc(logits_ready, 1)
                dve.wait_ge(logits_ready, n)
                nc.vector.reduce_max(top[:, :], logits, AX_X).then_inc(top_ready, 1)
                nc.vector.tensor_tensor(ties[:, :, :], other, here, ALU.is_equal).then_inc(compared, 1)
                dve.wait_ge(top_ready, n)
                nc.vector.tensor_scalar(below[:, :], logits, top[:, :], None, ALU.subtract).then_inc(below_ready, 1)
                nc.vector.tensor_tensor(greater[:, :, :], other, here, ALU.is_gt).then_inc(compared, 1)
                dve.wait_ge(compared, 2 * n)
                nc.vector.tensor_tensor(ties[:, :, :], ties[:, :, :], earlier[:, :, :], ALU.mult) \
                    .then_inc(ties_ready, 1)
                dve.wait_ge(ties_ready, n)
                nc.vector.tensor_tensor(greater[:, :, :], greater[:, :, :], ties[:, :, :], ALU.add) \
                    .then_inc(ahead_ready, 1)
                dve.wait_ge(ahead_ready, n)
                nc.vector.reduce_sum(rank[:, :], greater[:, :, :], AX_X).then_inc(rank_ready, 1)
                dve.wait_ge(rank_ready, n)
                dve.wait_ge(exp_ready, n)
                nc.vector.scalar_tensor_tensor(out=chosen[:, :], in0=rank[:, :], scalar=float(TOP_K), in1=exps[:, :],
                                               op0=ALU.is_lt, op1=ALU.mult).then_inc(chosen_ready, 1)
                dve.wait_ge(chosen_ready, n)
                nc.vector.reduce_sum(sum_exps[:, :], chosen[:, :], AX_X).then_inc(sum_exps_ready, 1)
                dve.wait_ge(sum_exps_ready, n)
                nc.vector.reciprocal(scale[:, :], sum_exps[:, :]).then_inc(scale_ready, 1)
                dve.wait_ge(scale_ready, n)
                nc.vector.tensor_scalar(gate[:, :], chosen[:, :], scale[:, :], SCALING, ALU.mult, ALU.mult) \
                    .then_inc(gate_ready, 1)
                dve.wait_ge(gate_ready, n)
                if c >= 1:
                    dve.wait_ge(lowT_done, n - 1)
                nc.vector.tensor_tensor(low[:, :].rearrange("p (e r) -> p e r", r=RANK),
                                        acc[:, c % 2, 2, RANKS[0]:RANKS[1]].rearrange("p (e r) -> p e r", r=RANK),
                                        gate[:, :].unsqueeze(2).broadcast_to([P, NE, RANK]), ALU.mult) \
                    .then_inc(low_ready, 1)

            def lowT_low(j, c):
                n = 4 * j + c + 1
                dve.wait_ge(lowT_hi_ready, n)
                nc.vector.tensor_tensor(lowT_lo[:, :], mixed[:, 0, 0:P], lowT_hi[:, :].bitcast(F32), ALU.subtract) \
                    .then_inc(lowT_ready, 1)

            def finish(j, c):
                n = 4 * j + c + 1
                dve.wait_ge(lora_done, n)
                dve.wait_ge(sum_ready, n)
                add_bank(c, slice(0, 2))
                add_bank(c, 2).then_inc(res_ready, 1)

            def add_bank(c, b):
                if type(b) is slice:
                    part = res[:, c % 4, 0:2 * BW].rearrange("p (b m) -> p b m", b=2)
                    return nc.vector.tensor_tensor(part, acc[:, c % 2, b, 0:BW], part, ALU.add)
                lo, hi = BANKS[b][0], min(BANKS[b][1], O)
                part = res[:, c % 4, lo:hi]
                return nc.vector.tensor_tensor(part, acc[:, c % 2, b, 0:hi - lo], part, ALU.add)

            for k in range(KT):
                if k == 0:
                    y_low(0, 0, 0)
                if k == 1:
                    y_low(0, 0, 1)
                dve.wait_ge(w_hi_ready, k + 1)
                nc.vector.tensor_tensor(w_lo[:, k, :], w_raw[:, k % STAGES, :], w_hi[:, k, :].bitcast(F32),
                                        ALU.subtract).then_inc(w_ready, 1)

            y_low(0, 1, 0)
            y_low(0, 1, 1)
            x_low(0, 2)
            dve.wait_ge(lb_hi_ready, 1)
            nc.vector.tensor_tensor(lb_lo[:, :], lb_raw[:, :], lb_hi[:, :].bitcast(F32), ALU.subtract) \
                .then_inc(lb_ready, 1)
            dve.wait_ge(consts_ready, NE)

            def step(j, c, split=True, ahead=True):
                gating(j, c - 1)
                if ahead:
                    turn(j, c + 1)
                lowT_low(j, c - 1)
                if ahead:
                    y_low(j, c + 1, 0)
                    y_low(j, c + 1, 1)
                finish(j, c - 1)
                if split:
                    x_low(j, c + 2)

            step(0, 1)
            with dve.Fori(0, LOOPS) as j:
                for u in (2, 3, 4, 5):
                    step(j, u)
            step(0, PAIRS - 2, split=False)
            step(0, PAIRS - 1, split=False, ahead=False)
            gating(0, PAIRS - 1)
            lowT_low(0, PAIRS - 1)
            dve.wait_ge(lora_done, PAIRS)
            dve.wait_ge(sum_ready, PAIRS)
            add_bank(PAIRS - 1, 2)
            add_bank(PAIRS - 1, 0).then_inc(res_ready, 1)
            dve.wait_ge(lora_done, PAIRS + 1)
            add_bank(PAIRS - 1, 1).then_inc(res_ready, 1)

        @block.tensor
        def _(pe):
            PRODUCTS = [(y_hi, w_hi), (y_hi, w_lo), (y_lo, w_hi)]

            def project(c, k, b, product):
                y_part, w_part = PRODUCTS[product]
                lo, hi = BANKS[b]
                return nc.tensor.matmul(acc[:, c % 2, b, 0:hi - lo], y_part[:, c % 2, k, :], w_part[:, k, lo:hi],
                                        start=(k == 0 and product == 0), stop=(k == KT - 1 and product == 2))

            def mix_early(c, h):
                if h == 0:
                    pe.wait_ge(x_in[c], 16)
                    pe.wait_ge(sel_ready, 2 * c + 2)
                x_blocks = x_sb[:, c, :].rearrange("p (m k) -> p k m", k=KT)
                for k in range(HALF_K):
                    last = nc.tensor.matmul(mixed[:, h, k * P:(k + 1) * P], x_blocks[:, h * HALF_K + k, :],
                                            w_pair[:, c, :], start=True, stop=True)
                last.then_inc(mix_done, 1)

            def mix(j, c):
                n = 4 * j + c
                pe.wait_ge(x_split, n - 1)
                pe.wait_ge(sel_ready, 2 * n + 2)
                if c >= 3:
                    pe.wait_ge(moved, 2 * (n - 2))
                    pe.wait_ge(lowT_ready, n - 2)
                for h in range(2):
                    for w_part, x_part in ((0, 0), (0, 1), (1, 0)):
                        last = nc.tensor.matmul(mixed[:, h, :], w_sel[:, c % 2, w_part, :],
                                                x_parts[:, x_part, h * 512:(h + 1) * 512],
                                                start=(w_part + x_part == 0), stop=(w_part == 1))
                    last.then_inc(mix_done, 1)

            def transpose_low(j, c):
                pe.wait_ge(low_ready, 4 * j + c + 1)
                nc.tensor.transpose(mixed[:, 0, 0:P], low[:, :], ident[:, :]).then_inc(lowT_done, 1)

            def experts(c, b):
                lo, hi = BANKS[b][0], min(BANKS[b][1], O)
                for low_part, lb_part in ((lowT_hi, lb_hi), (lowT_hi, lb_lo), (lowT_lo, lb_hi)):
                    last = nc.tensor.matmul(acc[:, c % 2, b, 0:hi - lo], low_part[:, :], lb_part[:, lo:hi],
                                            start=False, stop=(low_part is lowT_lo), skip_group_check=True)
                return last

            def first_step():
                for k in range(KT):
                    if k % HALF_K == 0:
                        pe.wait_ge(y_hi_ready, k // HALF_K + 1)
                    pe.wait_ge(w_hi_ready, k + 1)
                    for b in range(3):
                        project(0, k, b, 0)
                    pe.wait_ge(w_ready, k + 1)
                    for b in range(3):
                        project(0, k, b, 1)
                    if k % HALF_K == 0:
                        pe.wait_ge(y_ready, k // HALF_K + 1)
                    for b in range(3):
                        done = project(0, k, b, 2)
                    if k == 5:
                        mix_early(1, 0)
                    if k == 6:
                        mix_early(1, 1)
                done.then_inc(proj_done, 1)

            def step(j, c):
                s = 4 * j + c
                if c >= 2:
                    mix(j, c + 1)
                    pe.wait_ge(res_ready, s - 1)
                for k in range(KT):
                    if k % HALF_K == 0:
                        pe.wait_ge(y_ready, 2 * s + k // HALF_K + 1)
                    for product in range(3):
                        for b in range(3):
                            done = project(c, k, b, product)
                    if k == 1 and c == 1:
                        mix(j, c + 1)
                    if k == 3:
                        pe.wait_ge(moved, 2 * (s - 1) + 1)
                        transpose_low(j, c - 1)
                    if k == 5:
                        if c == 1:
                            pe.wait_ge(lb_ready, 1)
                        pe.wait_ge(lowT_ready, s)
                        for b in range(3):
                            last = experts(c - 1, b)
                        last.then_inc(lora_done, 1)
                done.then_inc(proj_done, 1)

            def last_step(c):
                pe.wait_ge(res_ready, c - 1)
                pe.wait_ge(y_ready, 2 * c + 2)
                for b in (2, 0, 1):
                    for k in range(KT):
                        for product in range(3):
                            done = project(c, k, b, product)
                        if b == 2 and k == 5:
                            transpose_low(0, c - 1)
                        if b == 1 and k == 0:
                            transpose_low(0, c)
                        if b == 1 and k == 4:
                            pe.wait_ge(lowT_ready, c + 1)
                            experts(c, 2)
                            experts(c, 0).then_inc(lora_done, 1)
                    if b == 2:
                        done.then_inc(proj_done, 1)
                        pe.wait_ge(lowT_ready, c)
                        for before in range(3):
                            last = experts(c - 1, before)
                        last.then_inc(lora_done, 1)
                    if b == 1:
                        experts(c, 1).then_inc(lora_done, 1)

            pe.wait_ge(consts_ready, NE)
            mix_early(0, 0)
            mix_early(0, 1)
            first_step()
            step(0, 1)
            with pe.Fori(0, LOOPS) as j:
                for u in (2, 3, 4, 5):
                    step(j, u)
            step(0, PAIRS - 2)
            last_step(PAIRS - 1)


def kernel(**inputs):
    import numpy as np
    import concourse.bacc as bacc
    from concourse.bass_utils import run_bass_kernel_spmd

    x = np.ascontiguousarray(inputs["x"])
    lora_a = np.asarray(inputs["L0_ffn_lora_A"])
    E, R, T = lora_a.shape
    base_w = np.asarray(inputs["L0_ffn_base_w"])
    cond_w = np.asarray(inputs["L0_cond_weights"])
    arrays = {
        "x": x,
        "condition": np.ascontiguousarray(inputs["itok_B_0_15"]).reshape(1, -1),
        "cond_w": np.ascontiguousarray(cond_w.transpose(1, 0, 2)).reshape(cond_w.shape[1], -1),
        "proj_w": np.ascontiguousarray(np.concatenate(
            [base_w, lora_a.reshape(E * R, T), np.asarray(inputs["L0_ffn_gate_w"])]).T),
        "lora_b": np.ascontiguousarray(np.asarray(inputs["L0_ffn_lora_B"]).transpose(0, 2, 1)).reshape(E * R, -1),
        "base_b": np.ascontiguousarray(inputs["L0_ffn_base_b"]),
    }
    nc = bacc.Bacc("TRN2", target_bir_lowering=False, num_devices=1)
    args = [nc.dram_tensor(f"in_{name}", a.shape, mybir.dt.from_np(a.dtype), kind="ExternalInput").ap()
            for name, a in arrays.items()]
    shape = (x.shape[0], x.shape[1], base_w.shape[0])
    out = nc.dram_tensor("out", shape, mybir.dt.float32, kind="ExternalOutput").ap()
    adaln_ffn_kernel(nc, *args, out)
    r = run_bass_kernel_spmd(nc, [{f"in_{name}": a for name, a in arrays.items()}], core_ids=[0])
    return r.results[0]["out"]
```
